# Optimizing a Trainium2 kernel written in Bass

```python
import numpy as np
import jax
import jax.numpy as jnp

def _softmax(x, axis=-1):
    return jax.nn.softmax(x, axis=axis)

def _gelu(x):
    return jax.nn.gelu(x, approximate=True)

def _silu(x):
    return jax.nn.silu(x)

def _sigmoid(x):
    return jax.nn.sigmoid(x)

def _layernorm(x, axis=-1, eps=1e-05):
    m = jnp.mean(x, axis=axis, keepdims=True)
    v = jnp.var(x, axis=axis, keepdims=True)
    return (x - m) / jnp.sqrt(v + eps)

def _scatter_add(tgt, idx, src, axis=0):
    return tgt.at[idx].add(src)

def _segment_sum(src, seg, n):
    return jax.ops.segment_sum(src, seg, n)
kernel_name = 'mk_seq_preln_d2_jaxref_r4_888953'

def setup_inputs(seed: int=0):
    np.random.seed(seed)
    _w = jnp.asarray

    def _L0_attn_setup():
        import jax, jax.numpy as jnp
        import numpy as np
        import math
        B, N, E, D = (4, 2048, 256, 64)
        key = jax.random.key(seed)
        kx, kq, kk, kv, ko = jax.random.split(key, 5)
        x = jax.random.normal(kx, (B, N, E), dtype=jnp.float32)
        wq = jnp.sign(jax.random.normal(kq, (D, E), dtype=jnp.float32)) / math.sqrt(E)
        wk = jnp.sign(jax.random.normal(kk, (D, E), dtype=jnp.float32)) / math.sqrt(E)
        wv = jnp.sign(jax.random.normal(kv, (D, E), dtype=jnp.float32)) / math.sqrt(E)
        wo = jnp.sign(jax.random.normal(ko, (E, D), dtype=jnp.float32)) / math.sqrt(D)
        return {'x': x, 'wq': wq, 'wk': wk, 'wv': wv, 'wo': wo}
    _L0_attn_in = _L0_attn_setup()

    def _L0_ffn_setup():
        import jax, jax.numpy as jnp
        import numpy as np
        HIDDEN = 256
        N_EXPERTS = 8
        TOP_K = 2
        INTER = 352
        N_SHARED = 2
        SCALE = 1.0
        key = jax.random.key(seed)
        ks = jax.random.split(key, 9)
        s_h = 1.0 / np.sqrt(HIDDEN)
        s_i = 1.0 / np.sqrt(INTER)
        x = jax.random.normal(ks[0], (2, 512, HIDDEN), dtype=jnp.float32)
        gate_w = jax.random.uniform(ks[1], (N_EXPERTS, HIDDEN), jnp.float32, -s_h, s_h)
        wg = jax.random.uniform(ks[2], (N_EXPERTS, HIDDEN, INTER), jnp.float32, -s_h, s_h)
        wu = jax.random.uniform(ks[3], (N_EXPERTS, HIDDEN, INTER), jnp.float32, -s_h, s_h)
        wd = jax.random.uniform(ks[4], (N_EXPERTS, INTER, HIDDEN), jnp.float32, -s_i, s_i)
        si = INTER * N_SHARED
        s_si = 1.0 / np.sqrt(si)
        swg = jax.random.uniform(ks[5], (HIDDEN, si), jnp.float32, -s_h, s_h)
        swu = jax.random.uniform(ks[6], (HIDDEN, si), jnp.float32, -s_h, s_h)
        swd = jax.random.uniform(ks[7], (si, HIDDEN), jnp.float32, -s_si, s_si)
        return {'x': x, 'gate_w': gate_w, 'wg': wg, 'wu': wu, 'wd': wd, 'swg': swg, 'swu': swu, 'swd': swd}
    _L0_ffn_in = _L0_ffn_setup()

    def _L1_attn_setup():
        import jax, jax.numpy as jnp
        import numpy as np
        EMB = 256
        HEADS = 16
        WINDOW = 128
        key = jax.random.key(seed)
        ks = jax.random.split(key, 9)
        B, N = (2, 512)
        s = 0.02
        f32 = jnp.float32
        return {'x': jax.random.normal(ks[0], (B, N, EMB), dtype=f32), 'Wq': jax.random.normal(ks[1], (EMB, EMB), dtype=f32) * s, 'bq': jnp.zeros((EMB,), dtype=f32), 'Wk': jax.random.normal(ks[2], (EMB, EMB), dtype=f32) * s, 'bk': jnp.zeros((EMB,), dtype=f32), 'Wv': jax.random.normal(ks[3], (EMB, EMB), dtype=f32) * s, 'bv': jnp.zeros((EMB,), dtype=f32), 'Wp': jax.random.normal(ks[4], (EMB, EMB), dtype=f32) * s, 'bp': jnp.zeros((EMB,), dtype=f32)}
    _L1_attn_in = _L1_attn_setup()

    def _L1_ffn_setup():
        import jax, jax.numpy as jnp
        import numpy as np
        D = 256
        H = 1024
        E = 8
        B, N = (2, 512)
        key = jax.random.key(seed)
        ks = jax.random.split(key, 5)
        x = jax.random.normal(ks[0], (B, N, D), dtype=jnp.float32)
        W1 = jax.random.normal(ks[1], (E, D, H), dtype=jnp.float32) / np.sqrt(D)
        W2 = jax.random.normal(ks[2], (E, H, D), dtype=jnp.float32) / np.sqrt(H)
        Wg = jax.random.normal(ks[3], (D, E), dtype=jnp.float32) / np.sqrt(D)
        bg = jax.random.normal(ks[4], (E,), dtype=jnp.float32) * 0.01
        return {'x': x, 'W1': W1, 'W2': W2, 'Wg': Wg, 'bg': bg}
    _L1_ffn_in = _L1_ffn_setup()
    _d = {'L0_attn_x': _L0_attn_in['x'], 'L0_attn_wq': _L0_attn_in['wq'], 'L0_attn_wk': _L0_attn_in['wk'], 'L0_attn_wv': _L0_attn_in['wv'], 'L0_attn_wo': _L0_attn_in['wo'], 'L0_ffn_gate_w': _L0_ffn_in['gate_w'], 'L0_ffn_wg': _L0_ffn_in['wg'], 'L0_ffn_wu': _L0_ffn_in['wu'], 'L0_ffn_wd': _L0_ffn_in['wd'], 'L0_ffn_swg': _L0_ffn_in['swg'], 'L0_ffn_swu': _L0_ffn_in['swu'], 'L0_ffn_swd': _L0_ffn_in['swd'], 'L1_attn_Wq': _L1_attn_in['Wq'], 'L1_attn_bq': _L1_attn_in['bq'], 'L1_attn_Wk': _L1_attn_in['Wk'], 'L1_attn_bk': _L1_attn_in['bk'], 'L1_attn_Wv': _L1_attn_in['Wv'], 'L1_attn_bv': _L1_attn_in['bv'], 'L1_attn_Wp': _L1_attn_in['Wp'], 'L1_attn_bp': _L1_attn_in['bp'], 'L1_ffn_W1': _L1_ffn_in['W1'], 'L1_ffn_W2': _L1_ffn_in['W2'], 'L1_ffn_Wg': _L1_ffn_in['Wg'], 'L1_ffn_bg': _L1_ffn_in['bg']}
    _x0 = _d['L0_attn_x']
    _d['L0_attn_x'] = jax.random.normal(jax.random.fold_in(jax.random.key(seed), 1), (8, 512, 256), dtype=_x0.dtype)
    del _x0
    return _d

def reference(L0_attn_x, L0_attn_wq, L0_attn_wk, L0_attn_wv, L0_attn_wo, L0_ffn_gate_w, L0_ffn_wg, L0_ffn_wu, L0_ffn_wd, L0_ffn_swg, L0_ffn_swu, L0_ffn_swd, L1_attn_Wq, L1_attn_bq, L1_attn_Wk, L1_attn_bk, L1_attn_Wv, L1_attn_bv, L1_attn_Wp, L1_attn_bp, L1_ffn_W1, L1_ffn_W2, L1_ffn_Wg, L1_ffn_bg):

    def _L0_attn_ref(x, wq, wk, wv, wo):
        import jax, jax.numpy as jnp
        import numpy as np
        import math
        B, N, E, D = (4, 2048, 256, 64)
        Q = jnp.einsum('bne,de->bnd', x, wq)
        K = jnp.einsum('bne,de->bnd', x, wk)
        V = jnp.einsum('bne,de->bnd', x, wv)
        energy = jnp.einsum('bnd,bne->bde', K, V)
        context = jnp.einsum('bnd,bde->bne', Q, energy)
        context = context * jnp.asarray(math.sqrt(3.0 / D), dtype=context.dtype)
        out = jnp.einsum('bnd,ed->bne', context, wo)
        return out

    def _L0_ffn_ref(x, gate_w, wg, wu, wd, swg, swu, swd):
        import jax, jax.numpy as jnp
        import numpy as np
        HIDDEN = 256
        N_EXPERTS = 8
        TOP_K = 2
        INTER = 352
        N_SHARED = 2
        SCALE = 1.0
        B, S, H = x.shape
        xf = x.reshape(-1, H)
        T = xf.shape[0]
        logits = xf.astype(jnp.float32) @ gate_w.astype(jnp.float32).T
        scores = jax.nn.softmax(logits, axis=-1)
        topw, topi = jax.lax.top_k(scores, TOP_K)
        denom = topw.sum(axis=-1, keepdims=True) + 1e-20
        topw = topw / denom * SCALE
        wdense = jnp.zeros((T, N_EXPERTS), jnp.float32).at[jnp.arange(T)[:, None], topi].set(topw)
        hg = jnp.einsum('th,ehi->eti', xf, wg)
        hu = jnp.einsum('th,ehi->eti', xf, wu)
        eo = jnp.einsum('eti,eih->eth', jax.nn.silu(hg) * hu, wd)
        y = jnp.einsum('te,eth->th', wdense, eo)
        shared = jax.nn.silu(xf @ swg) * (xf @ swu) @ swd
        return (y + shared).reshape(B, S, H)

    def _L1_attn_ref(x, Wq, bq, Wk, bk, Wv, bv, Wp, bp):
        import jax, jax.numpy as jnp
        import numpy as np
        EMB = 256
        HEADS = 16
        WINDOW = 128
        B, N, E = x.shape
        H = HEADS
        d = E // H

        def proj(W, b):
            y = jnp.einsum('bne,fe->bnf', x, W) + b
            return y.reshape(B, N, H, d).transpose(0, 2, 1, 3)
        q = proj(Wq, bq)
        k = proj(Wk, bk)
        v = proj(Wv, bv)
        energy = jnp.einsum('bhqd,bhkd->bhqk', q, k)
        idx = jnp.arange(N)
        out_of_window = jnp.abs(idx[:, None] - idx[None, :]) > WINDOW
        fmin = jnp.finfo(jnp.float32).min
        energy = jnp.where(out_of_window, fmin, energy)
        scaling = jnp.sqrt(jnp.float32(E))
        att = jax.nn.softmax(energy / scaling, axis=-1)
        out = jnp.einsum('bhqk,bhkd->bhqd', att, v)
        out = out.transpose(0, 2, 1, 3).reshape(B, N, E)
        return jnp.einsum('bne,fe->bnf', out, Wp) + bp

    def _L1_ffn_ref(x, W1, W2, Wg, bg):
        import jax, jax.numpy as jnp
        import numpy as np
        D = 256
        H = 1024
        E = 8
        B, N = (2, 512)
        b, n, d = x.shape
        e = Wg.shape[1]
        xf = x.reshape(b * n, d)
        logits = xf @ Wg + bg
        one_hot = jax.nn.one_hot(jnp.argmax(logits, axis=-1), e, dtype=x.dtype)
        h = jax.nn.gelu(jnp.einsum('td,edh->eth', xf, W1), approximate=True)
        y = jnp.einsum('eth,ehd->etd', h, W2)
        out = jnp.einsum('etd,te->td', y, one_hot)
        return out.reshape(b, n, d)
    x = L0_attn_x
    x = x + _L0_attn_ref(_layernorm(x, axis=-1), L0_attn_wq, L0_attn_wk, L0_attn_wv, L0_attn_wo)
    x = x + _L0_ffn_ref(_layernorm(x, axis=-1), L0_ffn_gate_w, L0_ffn_wg, L0_ffn_wu, L0_ffn_wd, L0_ffn_swg, L0_ffn_swu, L0_ffn_swd)
    x = x + _L1_attn_ref(_layernorm(x, axis=-1), L1_attn_Wq, L1_attn_bq, L1_attn_Wk, L1_attn_bk, L1_attn_Wv, L1_attn_bv, L1_attn_Wp, L1_attn_bp)
    x = x + _L1_ffn_ref(_layernorm(x, axis=-1), L1_ffn_W1, L1_ffn_W2, L1_ffn_Wg, L1_ffn_bg)
    return x

_drawn_inputs = setup_inputs


def setup_inputs(seed=0):
    import zlib

    import numpy as np

    out = dict(_drawn_inputs(seed))
    spreads = {'L1_attn_bq': (0.0, 2.0),
     'L1_attn_bk': (0.0, 2.0),
     'L1_attn_bv': (0.0, 0.8),
     'L1_attn_bp': (0.0, 2.0)}
    factors = {'L0_ffn_gate_w': 8.0,
     'L0_ffn_wg': 8.0,
     'L0_ffn_wu': 8.0,
     'L0_ffn_wd': 8.0,
     'L0_ffn_swg': 8.0,
     'L0_ffn_swu': 8.0,
     'L0_ffn_swd': 8.0,
     'L1_attn_Wq': 8.0,
     'L1_attn_Wk': 8.0,
     'L1_attn_Wv': 8.0,
     'L1_attn_Wp': 8.0,
     'L1_ffn_W1': 6.672,
     'L1_ffn_W2': 5.999,
     'L1_ffn_Wg': 6.311,
     'L1_ffn_bg': 8.0}
    for name, (base, spread) in spreads.items():
        noise = np.random.default_rng([zlib.crc32(name.encode()), seed]).standard_normal(out[name].shape)
        drawn = base * np.exp(spread * noise) if base else spread * noise
        out[name] = jnp.asarray(drawn.astype(out[name].dtype))
    for name, factor in factors.items():
        out[name] = (out[name] * factor).astype(out[name].dtype)
    return out
```

```python
from contextlib import ExitStack

import concourse.bass as bass
from concourse import mybir

F32 = mybir.dt.float32
F32R = mybir.dt.float32r
BF16 = mybir.dt.bfloat16
I32 = mybir.dt.int32
ALU = mybir.AluOpType
ACT = mybir.ActivationFunctionType
AX = mybir.AxisListType

P = 128
B, N, E = 8, 512, 256
TPB = N // P
NT = B * TPB
EC = E // P
D0 = 64
NX = 8
TOP0, TOP1 = 2, 1
INTER = 352
SI = 704
HID = 1024
NBLK0 = NT * TOP0 + NX - 1
NBLK1 = NT * TOP1 + NX - 1
H, DH = 16, 16
G = 4
SLOT = 64
EPS = 1e-5
MASKED = -3.0e38


class Lane:

    def __init__(self, sem):
        self.sem, self.count, self.todo, self.seen = sem, 0, [], {}

    def wait(self, *marks):
        for sem, value in marks:
            if self.seen.get(sem.name, 0) < value:
                self.seen[sem.name] = value
                self.todo.append(lambda e, sem=sem, value=value: e.wait_ge(sem, value))

    def do(self, emit):
        self.todo.append(emit)

    def mark(self, emit):
        self.count += 1
        self.todo.append(lambda e: emit(e).then_inc(self.sem, 1))
        return (self.sem, self.count)

    def dma(self, channel, emit):
        channel[1] += 16
        self.todo.append(lambda e: emit(e).then_inc(channel[0], 16))
        return (channel[0], channel[1])


class Ring:

    def __init__(self, slots, readers=None):
        self.slots, self.readers, self.at = slots, {} if readers is None else readers, 0
        self.taken = set()

    def take(self, lane):
        slot = self.slots[self.at % len(self.slots)]
        self.at += 1
        assert slot not in self.taken, slot
        self.taken.add(slot)
        for part in slot if isinstance(slot, tuple) else (slot,):
            lane.wait(*self.readers.get(part, ()))
        return slot

    def give(self, slot, *marks):
        self.taken.remove(slot)
        for part in slot if isinstance(slot, tuple) else (slot,):
            self.readers[part] = marks


def pipeline(n, steps):
    for t in range(n + len(steps) - 1):
        for k in reversed(range(len(steps))):
            if 0 <= t - k < n:
                steps[k](t - k)


def build(nc, a, out):
    ctx = ExitStack()
    with ctx:
        def sb(name, shape, dt=F32):
            return ctx.enter_context(nc.sbuf_tensor(name, shape, dt))

        def sem(name):
            return ctx.enter_context(nc.semaphore(name))

        def channel(name):
            return [sem(name), 0]

        X = sb("X", [P, NT, E])
        ARENA = 32768
        arena_at = nc.sbuf_base
        arena = sb("arena", [P, ARENA])

        def over(name, word, shape, dt):
            return nc.alloc_sbuf_tensor_at(name, shape, dt, offset=arena_at + 4 * word)

        q_rows = over("q_rows", 0, [P, 2, TPB, H * SLOT], F32R)
        k_rows = over("k_rows", 8192, [P, TPB, H * SLOT], F32R)
        qT = over("qT", 12288, [P, H // 2, N], F32R)
        kT = over("kT", 16384, [P, H // 2, N], F32R)
        work = sb("work", [P, 8192])
        ident = sb("ident", [P, P])
        before = sb("before", [P, P])
        ones = sb("ones", [P, P])
        mask = sb("mask", [P, 3 * P], BF16)
        logits = sb("logits", [P, NT, NX])
        w_gate = sb("w_gate", [P, 2, EC, NX])
        b_gate = sb("b_gate", [P, NX])
        b_qkv = sb("b_qkv", [P, 3 * E])
        b_p = sb("b_p", [P, E])
        stats = sb("stats", [P, 2 * TPB, 6])
        mv = sb("mv", [P, NT, 2])
        veps = sb("veps", [P, NT])
        rstd = sb("rstd", [P, NT])
        minus_half = sb("minus_half", [P, NT])
        restart = sb("restart", [P, NX, NT])
        descending = sb("descending", [P, NX])
        c_got = sb("c_got", [P, 2, E])
        blk_first = sb("blk_first", [P, NT])
        count = sb("count", [P, P])
        blk_no = count[:, 0:NBLK0]
        blk_expert = sb("blk_expert", [P, 2, NBLK0], I32)
        top_w = sb("top_w", [P, TOP0, NT])
        slot_of = sb("slot_of", [P, 3, NT], I32)
        iota_i = sb("iota_i", [P, P], I32)
        row_no = sb("row_no", [P, 1])
        token_of = sb("token_of", [P, 2, NBLK0], I32)
        token_out = sb("token_out", [P, NBLK1], I32)
        small = sb("small", [P, 12, NT])
        normed = [nc.dram_tensor(f"normed{l}", [NT * P, E], F32, kind="Internal").ap() for l in range(2)]
        resid = nc.dram_tensor("resid", [NT * P, E], F32, kind="Internal").ap()
        results = nc.dram_tensor("results", [NBLK0 * P, E], F32, kind="Internal").ap()
        psum = ctx.enter_context(nc.psum_tensor("psum", [P, 8, 512], F32))
        bank_readers = {}

        def banks(slots):
            return Ring(slots, bank_readers)

        block = ctx.enter_context(nc.Block())
        pe, act, dve, pool, sp = (Lane(sem(f"s_{n}")) for n in ("pe", "act", "dve", "pool", "sp"))
        c_x = [channel(f"c_x{b}") for b in range(B)]
        c_wa, c_bias, c_wu0, c_wd0, c_sh, c_wc = (
            channel(n) for n in ("c_wa", "c_bias", "c_wu0", "c_wd0", "c_sh", "c_wc"))
        c_w1 = [channel(f"c_w1{e}") for e in range(NX)]
        c_norm_out = [channel(f"c_norm{i}") for i in range(2)]
        c_resid = channel("c_resid")
        c_xrow = [channel(f"c_xrow{i}") for i in range(4)]
        c_rows = [channel(f"c_rows{i}") for i in range(3)]
        c_res = [channel(f"c_res{i}") for i in range(3)]
        c_gath = [channel(f"c_gath{i}") for i in range(TPB * TOP0)]
        c_out = [channel(f"c_out{i}") for i in range(3)]

        def carve(t, at, *shape):
            n = 1
            for s in shape:
                n *= s
            v = t[:, at:at + n]
            names = "abcd"[:len(shape)]
            if len(shape) > 1:
                v = v.rearrange(f"p ({' '.join(names)}) -> p {' '.join(names)}",
                                **{k: s for k, s in zip(names, shape)})
            return v

        wu0 = carve(arena, 0, NX, EC, 2 * INTER)
        DC = 3
        IC = [P, P, INTER - 2 * P]
        wd0 = carve(arena, 11264, NX, DC, E)
        sgu = carve(arena, 17408, EC, 2, SI)
        SC = [P] * 5 + [SI - 5 * P]
        sdn = carve(arena, 20224, len(SC), E)
        xnT_all = carve(arena, 21760, B, EC, N)
        w_qkv = carve(arena, 30720, EC, 3 * E)
        w_p = carve(arena, 30720 + 1536, EC, E)
        w12 = carve(arena, 0, NX, EC * HID + HID * E // P)
        w1 = w12[:, :, 0:EC * HID].rearrange("p x (c n) -> p x c n", c=EC)
        w2 = w12[:, :, EC * HID:].rearrange("p x (c n) -> p x c n", n=E)
        w_kv = carve(arena, 29952, EC, 2 * D0)
        w_q = carve(arena, 30208, EC, D0)
        w_o = arena[0:D0, 30336:30336 + E]
        xn = carve(work, 0, 2, TPB, E)
        xnT = carve(work, 2048, 2, EC, N)

        pool.do(lambda e: e.memset(minus_half[:, :], -0.5))
        made = pool.mark(lambda e: e.memset(ident[:, :], 0.0))
        pool.wait(made)
        k_ident = pool.mark(lambda e: e.affine_select(
            out=ident[:, :], in_=ident[:, :], compare_op=ALU.not_equal, fill=1.0, base=0,
            pattern=[[-1, P]], channel_multiplier=1))
        pool.do(lambda e: e.memset(ones[:, :], 1.0))
        pool.do(lambda e: e.memset(mask[:, :], 0.0))
        made = pool.mark(lambda e: e.memset(before[:, :], 1.0))
        pool.wait(made)
        pool.do(lambda e: e.affine_select(out=before[:, :], in_=before[:, :], compare_op=ALU.is_gt, fill=0.0,
                                          base=0, pattern=[[1, P]], channel_multiplier=-1))
        pool.do(lambda e: e.affine_select(out=mask[:, 0:P], in_=mask[:, 0:P], compare_op=ALU.is_ge,
                                          fill=MASKED, base=0, pattern=[[1, P]], channel_multiplier=-1))
        pool.do(lambda e: e.affine_select(out=mask[:, 2 * P:], in_=mask[:, 2 * P:], compare_op=ALU.is_ge,
                                          fill=MASKED, base=0, pattern=[[-1, P]], channel_multiplier=1))
        k_iota = pool.mark(lambda e: e.iota(iota_i[:, :], [[1, P]], base=0, channel_multiplier=0))
        dve.wait(k_iota)
        dve.do(lambda e: e.tensor_copy(count[:, :], iota_i[:, :]))
        made = pool.mark(lambda e: e.iota(token_of[:, 0, 0:1], [[1, 1]], base=0, channel_multiplier=1))
        dve.wait(made)
        dve.do(lambda e: e.tensor_copy(row_no[:, :], token_of[:, 0, 0:1]))
        made = dve.mark(lambda e: e.memset(restart[:, :, :], 1.0))
        dve.wait(made)
        dve.do(lambda e: e.memset(restart[:, :, 0:1], 0.0))
        dve.do(lambda e: e.tensor_scalar(blk_first[:, :], blk_no[:, 0:NT], float(P), None, ALU.mult))
        k_const = dve.mark(lambda e: e.tensor_scalar(descending[:, :], blk_no[:, 0:NX], -1.0, float(NX),
                                                     ALU.mult, ALU.add))

        x_in = a["x"].rearrange("b (t p) c -> p b t c", p=P)
        k_x = []
        for b in range(B):
            k_x.append(sp.dma(c_x[b], lambda e, b=b: e.dma_start(X[:, b * TPB:(b + 1) * TPB, :], x_in[:, b, :, :])))
        act.dma(c_wa, lambda e: e.dma_start(w_kv, a["wkvT"].rearrange("(c p) n -> p c n", p=P)))
        act.dma(c_wa, lambda e: e.dma_start(w_q, a["wqT"].rearrange("(c p) n -> p c n", p=P)))
        act.dma(c_wa, lambda e: e.dma_start(w_o, a["woT"]))
        for l, n in enumerate(("gate0T", "gate1")):
            k_wa = act.dma(c_wa, lambda e, l=l, n=n: e.dma_start(
                w_gate[:, l, :, :], a[n].rearrange("(c p) n -> p c n", p=P)))
        act.dma(c_bias, lambda e: e.dma_start(b_qkv[:, :], a["bqkv"].rearrange("(o n) -> o n", o=1).broadcast_to([P, 3 * E])))
        act.dma(c_bias, lambda e: e.dma_start(b_p[:, :], a["bp"].rearrange("(o n) -> o n", o=1).broadcast_to([P, E])))
        k_bias = act.dma(c_bias, lambda e: e.dma_start(b_gate[:, :], a["bg"].rearrange("(o n) -> o n", o=1).broadcast_to([P, NX])))
        for i, n in enumerate(("swg", "swu")):
            sp.dma(c_sh, lambda e, i=i, n=n: e.dma_start(sgu[:, :, i, :], a[n].rearrange("(c p) n -> p c n", p=P)))
        sp.dma(c_sh, lambda e: e.dma_start(sdn[:, 0:5, :], a["swd"][0:5 * P, :].rearrange("(c p) n -> p c n", p=P)))
        k_sh = sp.dma(c_sh, lambda e: e.dma_start(sdn[0:SC[5], 5, :], a["swd"][5 * P:SI, :]))
        for i, n in enumerate(("wg", "wu")):
            for c in range(EC):
                k_wu0 = sp.dma(c_wu0, lambda e, i=i, n=n, c=c: e.dma_start(
                    wu0[:, :, c, i * INTER:(i + 1) * INTER], a[n][:, c * P:(c + 1) * P, :].rearrange("x p n -> p x n")))
        for c in range(DC):
            k_wd0 = sp.dma(c_wd0, lambda e, c=c: e.dma_start(
                wd0[0:IC[c], :, c, :], a["wd"][:, c * P:c * P + IC[c], :].rearrange("x p n -> p x n")))
        k_rstd, k_stats = {}, {}
        k_resid = {t: k_x[t // TPB] for t in range(NT)}

        def norm_stats(b):
            for t in range(b * TPB, (b + 1) * TPB):
                tile_stats(t)
            norm_scale(b)

        def tile_stats(t):
            dve.wait(k_resid[t])
            k_stats[t] = dve.mark(lambda e: e.bn_stats(stats[:, t % (2 * TPB), :], X[:, t, :]))

        def norm_scale(b):
            ts = range(b * TPB, (b + 1) * TPB)
            dve.wait(k_stats[ts[-1]])
            for t in ts:
                m = dve.mark(lambda e, t=t: e.bn_aggr(mv[:, t, :], stats[:, t % (2 * TPB), :]))
            dve.wait(m)
            s = slice(b * TPB, (b + 1) * TPB)
            m = dve.mark(lambda e: e.tensor_scalar(veps[:, s], mv[:, s, 1], EPS, None, ALU.add))
            pool.wait(m)
            k_rstd[b] = pool.mark(lambda e: e.tensor_tensor(rstd[:, s], veps[:, s], minus_half[:, s], ALU.pow))

        def norm_apply(t, dst):
            dve.wait(k_rstd[t // TPB])
            return dve.mark(lambda e: e.tensor_scalar(dst, X[:, t, :], mv[:, t, 0:1], rstd[:, t:t + 1],
                                                      ALU.subtract, ALU.mult))

        xn_ring = Ring([0, 1])
        a_banks = tr_banks = banks([6, 7])
        xnT_ring = Ring([0, 1])

        def norm_batch(b, ring):
            s = ring.take(dve)
            for t in range(TPB):
                m = norm_apply(b * TPB + t, xn[:, s, t, :])
            return s, m

        def keep_normed(l, b, s, k):
            sp.wait(k)
            return sp.dma(c_norm_out[s], lambda e: e.dma_start(
                normed[l].rearrange("(b t p) c -> p b t c", p=P, t=TPB)[:, b, :, :], xn[:, s, :, :]))

        def transpose_batch(s, k_xn, dst, ring_of_banks, ring, *others):
            pe.wait(k_ident, k_xn)
            marks = []
            for c in range(EC):
                bk = ring_of_banks.take(pe)
                for t in range(TPB):
                    emit = lambda e, bk=bk, t=t, c=c: e.transpose(
                        psum[:, bk, t * P:(t + 1) * P], xn[:, s, t, c * P:(c + 1) * P], ident[:, :])
                    m = pe.mark(emit) if t == TPB - 1 else pe.do(emit)
                lane = (act, dve)[c]
                lane.wait(m)
                if c == 0:
                    k = act.mark(lambda e, bk=bk, c=c: e.activation(dst[:, c, :], psum[:, bk, :], ACT.Copy))
                else:
                    k = dve.mark(lambda e, bk=bk, c=c: e.tensor_copy(dst[:, c, :], psum[:, bk, :]))
                ring_of_banks.give(bk, k)
                marks.append(k)
            ring.give(s, m, *others)
            return marks

        kv_sb = carve(work, 4096, 2, TPB, 2 * D0)
        qT_sb = carve(arena, 30720, 4, N)
        en_sb = carve(arena, 30592, 2, D0)
        ew_sb = carve(work, 6144, 2, E)
        st = [dict() for _ in range(B)]
        scale = (3.0 / D0) ** 0.5
        kv_readers, en_readers, ew_readers = (Ring([0, 1]) for _ in range(3))
        qT_readers = Ring([0, 1, 2, 3])

        def a_norm(b):
            st[b]["xn"] = norm_batch(b, xn_ring)

        def a_turn(b):
            s, k = st[b]["xn"]
            xs = xnT_ring.take(act)
            dve.wait(*xnT_ring.readers.get(xs, ()))
            st[b]["xnT"] = xs, transpose_batch(s, k, xnT[:, xs, :, :], tr_banks, xn_ring)

        def a_qkv(b):
            xs, ks = st[b]["xnT"]
            pe.wait(k_wa, *ks)
            bk = a_banks.take(pe)
            for t in range(TPB):
                for c in range(EC):
                    emit = lambda e, t=t, c=c: e.matmul(
                        psum[:, bk, t * P:(t + 1) * P], xnT[:, xs, c, t * P:(t + 1) * P], w_kv[:, c, :],
                        start=(c == 0), stop=(c == EC - 1))
                    m = pe.mark(emit) if (t, c) == (TPB - 1, EC - 1) else pe.do(emit)
            s = kv_readers.take(act)
            act.wait(m)
            k = act.mark(lambda e: e.activation(kv_sb[:, s, :, :], psum[:, bk, :], ACT.Copy))
            a_banks.give(bk, k)
            st[b]["kv"] = s, k
            bq = a_banks.take(pe)
            for c in range(EC):
                emit = lambda e, c=c: e.matmul(psum[0:D0, bq, :], w_q[:, c, :], xnT[:, xs, c, :],
                                               start=(c == 0), stop=(c == EC - 1))
                m = pe.mark(emit) if c else pe.do(emit)
            xnT_ring.give(xs, m)
            qs = qT_readers.take(dve)
            dve.wait(m)
            k = dve.mark(lambda e: e.tensor_copy(qT_sb[0:D0, qs, :], psum[0:D0, bq, :]))
            a_banks.give(bq, k)
            st[b]["qT"] = qs, k

        def a_energy(b):
            s, k = st[b]["kv"]
            pe.wait(k)
            bk = a_banks.take(pe)
            for t in range(TPB):
                emit = lambda e, t=t: e.matmul(psum[0:D0, bk, 0:D0], kv_sb[:, s, t, D0:2 * D0], kv_sb[:, s, t, 0:D0],
                                               start=(t == 0), stop=(t == TPB - 1))
                m = pe.mark(emit) if t == TPB - 1 else pe.do(emit)
            kv_readers.give(s, m)
            q = en_readers.take(act)
            act.wait(m)
            k = act.mark(lambda e: e.activation(en_sb[0:D0, q, :], psum[0:D0, bk, 0:D0], ACT.Copy))
            a_banks.give(bk, k)
            st[b]["en"] = q, k

        def a_fold(b):
            s, k = st[b]["en"]
            pe.wait(k)
            bk = a_banks.take(pe)
            m = pe.mark(lambda e: e.matmul(psum[0:D0, bk, 0:E], en_sb[0:D0, s, :], w_o, start=True, stop=True))
            en_readers.give(s, m)
            q = ew_readers.take(act)
            act.wait(m)
            k = act.mark(lambda e: e.activation(ew_sb[0:D0, q, :], psum[0:D0, bk, 0:E], ACT.Copy, scale=scale))
            a_banks.give(bk, k)
            st[b]["ew"] = q, k

        def a_out(b):
            s, k = st[b]["ew"]
            qs, kq = st[b]["qT"]
            pe.wait(k, kq)
            for h in range(TPB // 2):
                bk = a_banks.take(pe)
                for u in range(2):
                    t = 2 * h + u
                    emit = lambda e, t=t, u=u, bk=bk: e.matmul(
                        psum[:, bk, u * E:(u + 1) * E], qT_sb[0:D0, qs, t * P:(t + 1) * P], ew_sb[0:D0, s, :],
                        start=True, stop=True)
                    m = pe.mark(emit) if u else pe.do(emit)
                t0 = b * TPB + 2 * h
                dve.wait(m)
                k = dve.mark(lambda e, t0=t0, bk=bk: e.tensor_tensor(
                    X[:, t0:t0 + 2, :], X[:, t0:t0 + 2, :],
                    psum[:, bk, :].rearrange("p (t c) -> p t c", t=2), ALU.add))
                a_banks.give(bk, k)
                k_resid[t0] = k_resid[t0 + 1] = k
            ew_readers.give(s, m)
            qT_readers.give(qs, m)

        def gate(l, b, src, ks, ring):
            pe.wait(k_wa, *ks)
            bk = ring.take(pe)
            for t in range(TPB):
                for c in range(EC):
                    emit = lambda e, t=t, c=c: e.matmul(
                        psum[:, bk, t * NX:(t + 1) * NX], src[:, c, t * P:(t + 1) * P], w_gate[:, l, c, :],
                        start=(c == 0), stop=(c == EC - 1))
                    m = pe.mark(emit) if (t, c) == (TPB - 1, EC - 1) else pe.do(emit)
            dve.wait(m)
            k = dve.mark(lambda e: e.tensor_copy(
                logits[:, b * TPB:(b + 1) * TPB, :], psum[:, bk, 0:TPB * NX].rearrange("p (t x) -> p t x", x=NX)))
            ring.give(bk, k)
            return m, k

        def m_norm(b):
            s, k = norm_batch(b, xn_ring)
            st[b]["xn2"] = s, k, keep_normed(0, b, s, k)

        def m_turn(b):
            s, k, kept = st[b]["xn2"]
            st[b]["kept"] = kept
            st[b]["xnT_all"] = transpose_batch(s, k, xnT_all[:, b, :, :], tr_banks, xn_ring, kept)

        def m_gate(b):
            st[b]["gate"] = gate(0, b, xnT_all[:, b, :, :], st[b]["xnT_all"], a_banks)[1]

        found = {}
        ROUTE_STEPS = 3

        def route(l, k_logits, ring, at):
            top, nblk = (TOP0, TOP1)[l], (NBLK0, NBLK1)[l]
            names = ["lg", "sc", "eq", "cand", "hot0", "hot1", "tot", "incl", "slot"]
            v = {n: carve(work, at + 256 * i, NT, NX) for i, n in enumerate(names[:8])}
            sm = lambda i: small[:, i, :]
            wide = lambda s: s.rearrange("p (t o) -> p t o", o=1).broadcast_to([P, NT, NX])
            each = lambda s: s.rearrange("p (o x) -> p o x", o=1).broadcast_to([P, NT, NX])

            def step(emit):
                m = dve.mark(emit)
                dve.wait(m)
                return m

            dve.wait(k_logits, k_const, k_bias)
            if l == 0:
                step(lambda e: e.tensor_reduce(sm(0), logits[:, :, :], AX.X, ALU.max))
                yield
                k = step(lambda e: e.tensor_tensor(v["lg"], logits[:, :, :], wide(sm(0)), ALU.subtract))
                yield
                act.wait(k)
                k = act.mark(lambda e: e.activation(v["sc"], v["lg"], ACT.Exp))
                dve.wait(k)
                step(lambda e: e.tensor_reduce(sm(1), v["sc"], AX.X, ALU.add))
                yield
                step(lambda e: e.reciprocal(sm(2), sm(1)))
                yield
                step(lambda e: e.tensor_tensor(v["sc"], v["sc"], wide(sm(2)), ALU.mult))
                yield
            else:
                step(lambda e: e.tensor_tensor(v["sc"], logits[:, :, :], each(b_gate[:, :]), ALU.add))
                yield
            for j in range(top):
                hot = f"hot{j}"
                step(lambda e, j=j: e.tensor_reduce(sm(3 + j), v["sc"], AX.X, ALU.max))
                yield
                step(lambda e, j=j: e.tensor_tensor(v["eq"], v["sc"], wide(sm(3 + j)), ALU.is_equal))
                yield
                step(lambda e: e.tensor_tensor(v["cand"], v["eq"], each(descending[:, :]), ALU.mult))
                yield
                step(lambda e: e.tensor_reduce(sm(5), v["cand"], AX.X, ALU.max))
                yield
                k = step(lambda e, hot=hot: e.tensor_tensor(v[hot], v["cand"], wide(sm(5)), ALU.is_equal))
                yield
                if j + 1 < top:
                    step(lambda e, hot=hot: e.scalar_tensor_tensor(v["sc"], v[hot], -4.0, v["sc"], ALU.mult, ALU.add))
                    yield
            if top == 2:
                k = step(lambda e: e.tensor_tensor(v["eq"], v["hot0"], v["hot1"], ALU.add))
                yield
                step(lambda e: e.tensor_tensor(sm(6), sm(3), sm(4), ALU.add))
                yield
                step(lambda e: e.tensor_scalar(sm(6), sm(6), 1e-20, None, ALU.add))
                yield
                step(lambda e: e.reciprocal(sm(7), sm(6)))
                yield
                step(lambda e: e.tensor_tensor(top_w[:, 0, :], sm(3), sm(7), ALU.mult))
                yield
                step(lambda e: e.tensor_tensor(top_w[:, 1, :], sm(4), sm(7), ALU.mult))
                yield
                chosen = v["eq"]
            else:
                chosen = v["hot0"]
            for _ in range(ROUTE_STEPS):
                yield
            pe.wait(k)
            k_bank = ring.take(pe)
            flat = chosen.rearrange("p t x -> p (t x)")
            pe.do(lambda e: e.matmul(psum[:, k_bank, 0:256], before[:, :], flat, start=True, stop=True))
            k = pe.mark(lambda e: e.matmul(psum[:, k_bank, 256:512], ones[:, :], flat, start=True, stop=True))
            dve.wait(k)
            tot = carve(work, at + 256 * 6, NX, NT)
            incl = carve(work, at + 256 * 7, NX, NT)
            rank = psum[:, k_bank, 0:256].rearrange("p (t x) -> p t x", x=NX)
            step(lambda e: e.tensor_copy(tot, psum[:, k_bank, 256:512].rearrange("p (t x) -> p x t", x=NX)))
            yield
            step(lambda e: e.tensor_tensor_scan(
                incl.rearrange("p x t -> p (x t)"), restart[:, :, :].rearrange("p x t -> p (x t)"),
                tot.rearrange("p x t -> p (x t)"), 0.0, ALU.mult, ALU.add))
            yield
            step(lambda e: e.tensor_tensor(tot, incl, tot, ALU.subtract))
            yield
            cmp = carve(work, at + 256 * 3, NX, NT)
            n_x = small[:, 8, 0:NX]
            step(lambda e: e.tensor_tensor(
                cmp, blk_first[:, :].rearrange("p (o t) -> p o t", o=1).broadcast_to([P, NX, NT]),
                incl[:, :, NT - 1:NT].broadcast_to([P, NX, NT]), ALU.is_lt))
            yield
            step(lambda e: e.tensor_reduce(n_x, cmp, AX.X, ALU.add))
            yield
            step(lambda e: e.tensor_scalar(n_x, n_x, 1.0, None, ALU.max))
            yield
            upto = small[:, 9, 0:NX]
            step(lambda e: e.tensor_tensor_scan(upto, ones[:, 0:NX], n_x, 0.0, ALU.mult, ALU.add))
            yield
            first = small[:, 10, 0:NX]
            step(lambda e: e.tensor_tensor(first, upto, n_x, ALU.subtract))
            yield
            step(lambda e: e.tensor_scalar(first, first, float(P), None, ALU.mult))
            yield
            step(lambda e: e.tensor_tensor(tot, tot, first.rearrange("p (x o) -> p x o", o=1).broadcast_to([P, NX, NT]),
                                           ALU.add))
            yield
            slot = carve(work, at + 256 * 7, NT, NX)
            k = step(lambda e: e.tensor_tensor(slot, rank, tot.rearrange("p x t -> p t x"), ALU.add))
            yield
            ring.give(k_bank, k)
            for j in range(top):
                step(lambda e, j=j: e.tensor_tensor(v["cand"], slot, v[f"hot{j}"], ALU.mult))
                yield
                step(lambda e: e.tensor_reduce(sm(11), v["cand"], AX.X, ALU.add))
                yield
                k_slot = step(lambda e, j=j: e.tensor_copy(slot_of[:, (0, TOP0)[l] + j, :], sm(11)))
                yield
            ends = carve(work, at, nblk, NX)
            step(lambda e: e.tensor_tensor(
                ends, blk_no[:, 0:nblk].rearrange("p (b o) -> p b o", o=1).broadcast_to([P, nblk, NX]),
                upto.rearrange("p (o x) -> p o x", o=1).broadcast_to([P, nblk, NX]), ALU.is_ge))
            yield
            which = carve(work, at + 256 * 3, nblk)
            step(lambda e: e.tensor_reduce(which, ends, AX.X, ALU.add))
            yield
            k_expert = step(lambda e: e.tensor_scalar(blk_expert[:, l, 0:nblk], which, float(NX - 1), None, ALU.min))
            yield
            found["slot", l], found["expert", l] = k_slot, k_expert

        def invert(l, ring, at, kept):
            top, nblk = (TOP0, TOP1)[l], (NBLK0, NBLK1)[l]
            CH, PIECES, LAG = 4, 4, 2
            hot_r = [carve(work, at + i * CH * P // 2, CH * P // 2).bitcast(BF16)
                     .rearrange("p (t r) -> p t r", t=CH) for i in range(PIECES)]
            at_b = at + PIECES * CH * P // 2
            nb = CH * 3 * nblk // 2
            hot_b = [carve(work, at_b + i * nb, nb).bitcast(BF16)
                     .rearrange("p (t k b) -> p t k b", t=CH, k=3) for i in range(PIECES)]
            part = small[:, 0:4, :]
            bk = ring.take(pe)
            piece = Ring(list(range(PIECES)))
            k_slot = found["slot", l]
            dve.wait(*kept)
            last = (top - 1, NT // CH - 1)
            built, produced = [], []

            def product(j, q, s, kc):
                pe.wait(kc)
                for t in range(CH):
                    first, final = (j, q, t) == (0, 0, 0), (j, q, t) == (*last, CH - 1)
                    emit = lambda e, t=t, first=first, final=final: e.matmul(
                        psum[:, bk, 0:3 * nblk], hot_r[s][:, t, :], hot_b[s][:, t, :, :].rearrange("p k b -> p (k b)"),
                        start=first, stop=final)
                    m = pe.mark(emit) if t == CH - 1 else pe.do(emit)
                piece.give(s, m)
                produced.append(m)

            for j in range(top):
                col = (0, TOP0)[l] + j
                dve.wait(k_slot)
                ints = [part[:, i, :].bitcast(I32) for i in range(2)]
                dve.do(lambda e, col=col: e.tensor_scalar(ints[0], slot_of[:, col, :], P - 1, None, ALU.bitwise_and))
                k = dve.mark(lambda e, col=col: e.tensor_scalar(ints[1], slot_of[:, col, :], P.bit_length() - 1, None,
                                                                ALU.arith_shift_right))
                dve.wait(k)
                k = dve.mark(lambda e: e.tensor_copy(part[:, 2:4, :], part[:, 0:2, :].bitcast(I32)))
                dve.wait(k)
                for q in range(NT // CH):
                    s = piece.take(dve)
                    ts = slice(q * CH, (q + 1) * CH)
                    spread = lambda v, n: v.rearrange("p (t o) -> p t o", o=1).broadcast_to([P, CH, n])
                    repeat = lambda v: v.rearrange("p (o n) -> p o n", o=1).broadcast_to([P, CH, v.shape[1]])
                    dve.do(lambda e, s=s, ts=ts: e.tensor_tensor(
                        hot_r[s], repeat(count[:, :]), spread(part[:, 2, ts], P), ALU.is_equal))
                    k = dve.mark(lambda e, s=s, ts=ts: e.tensor_tensor(
                        hot_b[s][:, :, 2, :], repeat(blk_no[:, 0:nblk]), spread(part[:, 3, ts], nblk), ALU.is_equal))
                    dve.wait(k)
                    kb = dve.mark(lambda e, s=s, ts=ts: e.tensor_tensor(
                        hot_b[s][:, :, 0, :], hot_b[s][:, :, 2, :], spread(count[:, ts], nblk), ALU.mult))
                    kc = dve.mark(lambda e, s=s: e.tensor_scalar(
                        hot_b[s][:, :, 1, :], hot_b[s][:, :, 2, :], row_no[:, 0:1], None, ALU.mult))
                    built.append((j, q, s, kc))
                    if len(built) > LAG:
                        product(*built.pop(0))
                    yield
            for _ in range(LAG):
                yield
            while built:
                product(*built.pop(0))
            m = produced[-1]
            tile_no, row, taken = (psum[:, bk, i * nblk:(i + 1) * nblk] for i in range(3))
            f = [carve(work, at + i * P, nblk) for i in range(3)]
            dve.wait(m)
            k = dve.mark(lambda e: e.tensor_copy(f[0], row))
            dve.wait(k)
            k = dve.mark(lambda e: e.scalar_tensor_tensor(f[1], tile_no, float(P), f[0], ALU.mult, ALU.add))
            dve.wait(k)
            k_token = dve.mark(lambda e: e.tensor_copy(token_of[:, l, 0:nblk], f[1]))
            if l == 1:
                k = dve.mark(lambda e: e.scalar_tensor_tensor(f[2], taken, -float(2 * NT * P), f[1], ALU.mult, ALU.add))
                dve.wait(k)
                k = dve.mark(lambda e: e.tensor_scalar(f[2], f[2], float(2 * NT * P), None, ALU.add))
                dve.wait(k)
                k_token = dve.mark(lambda e: e.tensor_copy(token_out[:, :], f[2]))
            ring.give(bk, k_token)
            found["token", l] = k_token

        h_banks = banks([(2, 3), (4, 5)])
        y_banks = banks([(0, 1)])
        sil = carve(work, 5120, 2, N)
        aT_s = carve(work, 6656, 3, N)
        sil_ring, aT_ring = Ring([0, 1]), Ring([0, 1, 2])
        NC = len(SC)
        sh = {}

        def s_up(b, c):
            pe.wait(k_sh, *st[b]["xnT_all"])
            w = SC[c]
            pair = h_banks.take(pe)
            for u in range(2):
                for k in range(EC):
                    emit = lambda e, u=u, k=k: e.matmul(
                        psum[0:w, pair[u], :], sgu[:, k, u, c * P:c * P + w], xnT_all[:, b, k, :],
                        start=(k == 0), stop=(k == EC - 1))
                    m = pe.mark(emit) if k else pe.do(emit)
                if u == 0:
                    mg = m
            s = sil_ring.take(act)
            act.wait(mg)
            ka = act.mark(lambda e: e.activation(sil[0:w, s, :], psum[0:w, pair[0], :], ACT.Silu))
            q = aT_ring.take(dve)
            dve.wait(ka, m)
            kd = dve.mark(lambda e: e.tensor_tensor(aT_s[0:w, q, :], sil[0:w, s, :], psum[0:w, pair[1], :], ALU.mult))
            h_banks.give(pair, kd)
            sil_ring.give(s, kd)
            sh[b, c] = q, kd

        def s_down(b, c):
            q, k = sh[b, c]
            w = SC[c]
            if c == 0:
                sh["y", b] = y_banks.take(pe)
            ys = sh["y", b]
            pe.wait(k)
            for t in range(TPB):
                emit = lambda e, t=t: e.matmul(
                    psum[:, ys[t // 2], (t % 2) * E:(t % 2 + 1) * E], aT_s[0:w, q, t * P:(t + 1) * P], sdn[0:w, c, :],
                    start=(c == 0 and t % 2 == 0), stop=(c == NC - 1 and t % 2 == 1), skip_group_check=True)
                m = pe.mark(emit) if t == TPB - 1 else pe.do(emit)
            aT_ring.give(q, m)
            if c == NC - 1:
                dve.wait(m)
                t0 = b * TPB
                k = dve.mark(lambda e: e.tensor_tensor(
                    X[:, t0:t0 + TPB, :].rearrange("p t c -> p (t c)"), X[:, t0:t0 + TPB, :].rearrange("p t c -> p (t c)"),
                    psum[:, 0:2, :].rearrange("p a n -> p (a n)"), ALU.add))
                y_banks.give(ys, k)
                for t in range(TPB):
                    k_resid[t0 + t] = k

        def run(todo):
            for step in sorted(todo):
                for _, f, args in sorted(todo[step], key=lambda x: x[0]):
                    f(*args)

        def at(todo, step, rank, f, *args):
            todo.setdefault(step, []).append((rank, f, args))

        def load_attention_weights():
            sp.wait(*[m for marks in qT_readers.readers.values() for m in marks])
            sp.dma(c_wc, lambda e: e.dma_start(w_qkv, a["wqkvT"].rearrange("(c p) n -> p c n", p=P)))
            found["wc"] = sp.dma(c_wc, lambda e: e.dma_start(w_p, a["wpT"].rearrange("(c p) n -> p c n", p=P)))

        def find_rows(l, k_gate, ring, at_route, at_invert, kept):
            yield from route(l, k_gate, ring, at_route)
            yield from invert(l, ring, at_invert, kept)

        finder = []

        def find_some(n):
            if not finder:
                finder.append(find_rows(0, st[B - 1]["gate"], a_banks, 2048, 0, [st[b]["kept"] for b in (B - 2, B - 1)]))
            for _ in range(n):
                next(finder[0], None)

        ab = {}
        A_STEPS = [norm_stats, a_norm, a_turn, a_qkv, a_energy, a_fold, a_out, norm_stats, m_norm, m_turn, m_gate]
        PACE, LEAD = 3, 10
        for b in range(B):
            for k, f in enumerate(A_STEPS):
                at(ab, PACE * b + k, len(A_STEPS) - k, f, b)
            for c in range(NC):
                at(ab, LEAD + NC * b + c, 10, s_up, b, c)
                at(ab, LEAD + NC * b + c + 2, 0, s_down, b, c)
        routed_at = PACE * (B - 1) + len(A_STEPS)
        at(ab, routed_at, 20, load_attention_weights)
        for step in range(routed_at, LEAD + NC * B):
            at(ab, step, 20, find_some, ROUTE_STEPS if step < routed_at + 16 else 2)
        run(ab)
        for _ in finder[0]:
            pass
        k_wc, k_expert, k_token = found["wc"], found["expert", 0], found["token", 0]

        def load_rows(l, b, ring, xs, k_all):
            s = ring.take(pool)
            pool.wait(*k_all)
            return s, pool.dma(c_rows[s], lambda e: e.indirect_dma_start(
                out=xs[:, s, :], out_offset=None, in_=normed[l],
                in_offset=bass.IndirectOffsetOnAxis(ap=token_of[:, l, b:b + 1], axis=0)))

        def turn_rows(s, k, xs, xsT, bring, tring, ring):
            pe.wait(k)
            bk = bring.take(pe)
            for c in range(EC):
                emit = lambda e, c=c: e.transpose(psum[:, bk, c * P:(c + 1) * P], xs[:, s, c * P:(c + 1) * P], ident[:, :])
                m = pe.mark(emit) if c else pe.do(emit)
            ring.give(s, m)
            q = tring.take(act)
            act.wait(m)
            k = act.mark(lambda e: e.activation(xsT[:, q, :], psum[:, bk, 0:E], ACT.Copy))
            bring.give(bk, k)
            return q, k

        def keep_result(b, bk, m, y, y_ring, bring):
            s = y_ring.take(dve)
            dve.wait(m)
            k = dve.mark(lambda e: e.tensor_copy(y[:, s, :], psum[:, bk, 0:E]))
            bring.give(bk, k)
            sp.wait(k)
            k = sp.dma(c_res[s], lambda e: e.dma_start(results[b * P:(b + 1) * P, :], y[:, s, :]))
            y_ring.give(s, k)
            return k

        def experts0():
            xs = carve(work, 4096, 3, E)
            xsT = carve(work, 3072, 2, E)
            y = carve(work, 5376, 3, E)
            hsil = carve(work, 6144, 2, INTER)
            aT = carve(work, 6848, 2, DC * P)
            rx, rt, ry, rh, ra = Ring([0, 1, 2]), Ring([0, 1]), Ring([0, 1, 2]), Ring([0, 1]), Ring([0, 1])
            t_banks, u_banks, o_banks = banks([4, 5]), banks([(0, 1), (2, 3)]), banks([6, 7])
            it = [dict() for _ in range(NBLK0)]
            k_done = {}
            k_shared_done = k_resid[NT - 1]
            all_normed = [k_token] + [m for marks in kv_readers.readers.values() for m in marks]
            all_normed += [st[b]["kept"] for b in (B - 2, B - 1)]

            def load(b):
                it[b]["xs"] = load_rows(0, b, rx, xs, all_normed)

            def turn(b):
                it[b]["xsT"] = turn_rows(*it[b]["xs"], xs, xsT, t_banks, rt, rx)

            def up(b):
                q, k = it[b]["xsT"]
                pe.wait(k, k_wu0, k_expert)
                pair = u_banks.take(pe)

                def emit_up(e):
                    x = e.value_load(blk_expert[0:1, 0, b:b + 1], min_val=0, max_val=NX - 1)
                    for u in range(2):
                        for c in range(EC):
                            m = e.matmul(psum[:, pair[u], 0:INTER], xsT[:, q, c * P:(c + 1) * P],
                                         wu0[:, bass.ds(x, 1), c, u * INTER:(u + 1) * INTER],
                                         start=(c == 0), stop=(c == EC - 1))
                    return m
                m = pe.mark(emit_up)
                rt.give(q, m)
                s = rh.take(act)
                act.wait(m, k_shared_done)
                k = act.mark(lambda e: e.activation(hsil[:, s, :], psum[:, pair[0], 0:INTER], ACT.Silu))
                dve.wait(k)
                k = dve.mark(lambda e: e.tensor_tensor(hsil[:, s, :], hsil[:, s, :], psum[:, pair[1], 0:INTER], ALU.mult))
                u_banks.give(pair, k)
                it[b]["h"] = s, k

            def turn_h(b):
                s, k = it[b]["h"]
                pe.wait(k)
                bk = t_banks.take(pe)
                for c in range(DC):
                    emit = lambda e, c=c: e.transpose(psum[0:IC[c], bk, c * P:(c + 1) * P],
                                                      hsil[:, s, c * P:c * P + IC[c]], ident[:, :])
                    m = pe.mark(emit) if c == DC - 1 else pe.do(emit)
                rh.give(s, m)
                q = ra.take(dve)
                dve.wait(m)
                dve.do(lambda e: e.tensor_copy(aT[:, q, 0:2 * P], psum[:, bk, 0:2 * P]))
                k = dve.mark(lambda e: e.tensor_copy(aT[0:IC[2], q, 2 * P:3 * P], psum[0:IC[2], bk, 2 * P:3 * P]))
                t_banks.give(bk, k)
                it[b]["aT"] = q, k

            def down(b):
                q, k = it[b]["aT"]
                pe.wait(k, k_wd0)
                bk = o_banks.take(pe)

                def emit_down(e):
                    x = e.value_load(blk_expert[0:1, 0, b:b + 1], min_val=0, max_val=NX - 1)
                    for c in range(DC):
                        m = e.matmul(psum[:, bk, 0:E], aT[0:IC[c], q, c * P:(c + 1) * P],
                                     wd0[0:IC[c], bass.ds(x, 1), c, :], start=(c == 0), stop=(c == DC - 1))
                    return m
                m = pe.mark(emit_down)
                ra.give(q, m)
                it[b]["done"] = m
                k_done[b % 3] = keep_result(b, bk, m, y, ry, o_banks)

            pipeline(NBLK0, [load, lambda b: None, turn, up, turn_h, down])
            return list(k_done.values()), it[NBLK0 - 1]["done"]

        k_res0, k_experts0 = experts0()

        def fetch(t, j):
            if t < TPB:
                s, dst = TOP0 * t + j, first_got[:, TOP0 * t + j, :]
            else:
                s = got_ring.take(pool)
                dst = c_got[:, s, :]
            pool.wait(*k_res0, k_experts0)
            k = pool.dma(c_gath[s], lambda e: e.indirect_dma_start(
                out=dst, out_offset=None, in_=results,
                in_offset=bass.IndirectOffsetOnAxis(ap=slot_of[:, j, t:t + 1], axis=0)))
            got[t, j] = s, k, dst

        def add_fetched(t, j):
            s, k, src = got[t, j]
            dve.wait(k, k_resid[t])
            k = dve.mark(lambda e: e.scalar_tensor_tensor(
                X[:, t, :], src, top_w[:, j, t:t + 1], X[:, t, :], ALU.mult, ALU.add))
            if t >= TPB:
                got_ring.give(s, k)
            k_resid[t] = k
            if t == TPB - 1:
                k_first_added[:] = [k]

        k_first_added = []
        got, got_ring = {}, Ring([0, 1])
        first_got = carve(arena, 24576, TPB * TOP0, E)

        ROWS_S, ROWS_T = 3 * DH, 3 * DH + 2
        NG = H // G
        q_rowsv = q_rows[:, :, :, :].rearrange("p s t (h f) -> p s t h f", f=SLOT)
        k_rowsv = k_rows[:, :, :].rearrange("p t (h f) -> p t h f", f=SLOT)
        v32 = carve(arena, 20480, 2, TPB, H, 2 * DH)
        pT = carve(arena, 24576, 4, G, 3 * P)
        qk = carve(work, 4096, 2, 2 * E)
        masked = carve(work, 5120, 2 * 3 * P // 2).bitcast(BF16).rearrange("p (s n) -> p s n", s=2)
        masked_ring = Ring([0, 1])
        oT = carve(work, 5632, N)
        o = carve(work, 6144, TPB, E)
        oT2 = carve(work, 7168, EC, N)
        mx = small[:, 0:4, :].rearrange("p a b -> p (a b)").rearrange("p (s t h) -> p s t h", s=2, t=TPB)
        rec = small[:, 4, 0:TPB * G].rearrange("p (t g) -> p t g", t=TPB)
        s_banks = banks([0, 1, 2, 3, 4, 5, 6])
        O_BANK = banks([7])
        qkv_ring, pT_ring = Ring([0, 1]), Ring([0, 1, 2, 3])
        q_ring, k_ring, v_ring = Ring([0, 1]), Ring([0]), Ring([0, 1])
        o_ring, oT_ring, oT2_ring, rec_ring = (Ring([0]) for _ in range(4))
        ct = [dict() for _ in range(B)]
        un = [dict() for _ in range(B * NG)]

        def window(i):
            return max(i - 1, 0) * P, min(i + 2, TPB) * P

        act.wait(k_experts0)
        dve.wait(k_experts0)

        def fill_pads():
            pool.wait(k_experts0)
            for v in (k_rowsv, q_rowsv[:, 0], q_rowsv[:, 1]):
                made = pool.mark(lambda e, v=v: e.memset(v[:, :, :, ROWS_S:].bitcast(F32), 0.0))
            pool.do(lambda e: e.memset(v32[:, :, :, :, DH + 1:], 0.0))
            pool.wait(made)
            pool.do(lambda e: e.memset(v32[:, :, :, :, DH:DH + 1], 1.0))
            k_pads = pool.mark(lambda e: e.memset(k_rowsv[:, :, :, ROWS_S:ROWS_T].bitcast(F32), 1.0))
            act.wait(k_pads)
            dve.wait(k_pads)

        def c_norm(b, *tiles):
            if tiles[0] == 0:
                ct[b]["xn_slot"] = xn_ring.take(dve)
            s = ct[b]["xn_slot"]
            for t in tiles:
                k = norm_apply(b * TPB + t, xn[:, s, t, :])
            ct[b]["xn"] = s, k

        def c_turn(b):
            s, k = ct[b]["xn"]
            pool.wait(k, k_bias)
            t0 = b * TPB
            kb = pool.mark(lambda e: e.tensor_tensor(
                X[:, t0:t0 + TPB, :], X[:, t0:t0 + TPB, :],
                b_p[:, :].rearrange("p (o c) -> p o c", o=1).broadcast_to([P, TPB, E]), ALU.add))
            for t in range(TPB):
                k_resid[t0 + t] = kb
            xs = xnT_ring.take(act)
            dve.wait(*xnT_ring.readers.get(xs, ()))
            ct[b]["xnT"] = xs, transpose_batch(s, k, xnT[:, xs, :, :], s_banks, xn_ring)

        def c_qkv(b, t):
            xs, ks = ct[b]["xnT"]
            pe.wait(k_wc, *ks)
            if t == 0:
                ct[b]["q"], ct[b]["k"], ct[b]["v"] = q_ring.take(act), k_ring.take(act), v_ring.take(dve)
                dve.wait(*q_ring.readers.get(ct[b]["q"], ()), *k_ring.readers.get(0, ()))
            qs, vs = ct[b]["q"], ct[b]["v"]
            bqk, bv = s_banks.take(pe), s_banks.take(pe)
            for bk, n0, n1 in ((bqk, 0, 2 * E), (bv, 2 * E, 3 * E)):
                for c in range(EC):
                    emit = lambda e, bk=bk, n0=n0, n1=n1, c=c: e.matmul(
                        psum[:, bk, 0:n1 - n0], xnT[:, xs, c, t * P:(t + 1) * P], w_qkv[:, c, n0:n1],
                        start=(c == 0), stop=(c == EC - 1))
                    m = pe.mark(emit) if c else pe.do(emit)
                if bk == bqk:
                    mqk = m
            if t == TPB - 1:
                xnT_ring.give(xs, m)
            s = qkv_ring.take(dve)
            dve.wait(mqk, k_bias)
            k = dve.mark(lambda e: e.tensor_tensor(qk[:, s, :], psum[:, bqk, :], b_qkv[:, 0:2 * E], ALU.add))
            s_banks.give(bqk, k)
            dve.wait(m)
            heads = lambda v: v.rearrange("p (h d) -> p h d", d=DH)
            kv_done = dve.mark(lambda e: e.tensor_tensor(
                v32[:, vs, t, :, 0:DH], heads(psum[:, bv, 0:E]), heads(b_qkv[:, 2 * E:3 * E]), ALU.add))
            s_banks.give(bv, kv_done)
            q_in, k_in = heads(qk[:, s, 0:E]), heads(qk[:, s, E:2 * E])
            parts = lambda v: v[:, :, 0:3 * DH].rearrange("p h (s d) -> p h s d", d=DH)
            twice = lambda v: v.rearrange("p h (o d) -> p h o d", o=1).broadcast_to([P, H, 2, DH])
            qv, kv = parts(q_rowsv[:, qs, t, :, :]), parts(k_rowsv[:, t, :, :])
            act.wait(k)
            act.do(lambda e: e.activation(qv[:, :, 0:3:2, :], twice(q_in), ACT.Copy))
            ka = act.mark(lambda e: e.activation(kv[:, :, 0:2, :], twice(k_in), ACT.Copy))
            ct[b]["hi", t] = s, q_in, k_in, qv, kv, ka
            ct[b]["k_v"] = kv_done

        def c_low(b, t):
            s, q_in, k_in, qv, kv, ka = ct[b]["hi", t]
            dve.wait(ka)
            dve.do(lambda e: e.tensor_tensor(qv[:, :, 1, :], q_in, qv[:, :, 0, :].bitcast(F32), ALU.subtract))
            kd = dve.mark(lambda e: e.tensor_tensor(kv[:, :, 2, :], k_in, kv[:, :, 0, :].bitcast(F32), ALU.subtract))
            qkv_ring.give(s, ka, kd)
            ct[b]["rows"] = ka, kd

        def rows_to_cols(src, p, dst, lane):
            bk = s_banks.take(pe)
            for t in range(TPB):
                emit = lambda e, t=t: e.transpose(psum[:, bk, t * P:(t + 1) * P], src(t).bitcast(F32), ident[:, :])
                m = pe.mark(emit) if t == TPB - 1 else pe.do(emit)
            lane.wait(m)
            if lane is act:
                k = act.mark(lambda e: e.activation(dst[:, p, :], psum[:, bk, :], ACT.Copy))
            else:
                k = dve.mark(lambda e: e.tensor_copy(dst[:, p, :], psum[:, bk, :]))
            s_banks.give(bk, k)
            return m, k

        def u_cols(u, of, i):
            b, g = divmod(u, NG)
            p = 2 * g + i
            qs = ct[b]["q"]
            pe.wait(*ct[b]["rows"])
            lane = act if of == "k" else dve
            lane.wait(*cols_readers.get(g, ()))
            if of == "k":
                m, k = rows_to_cols(lambda t: k_rows[:, t, p * P:(p + 1) * P], p, kT, lane)
                if p == H // 2 - 1:
                    k_ring.give(ct[b]["k"], m)
            else:
                m, k = rows_to_cols(lambda t: q_rows[:, qs, t, p * P:(p + 1) * P], p, qT, lane)
            un[u].setdefault("cols", []).append(k)

        cols_readers = {}

        def u_scores(u, i, hd):
            b, g = divmod(u, NG)
            lo, hi = window(i)
            w, off = hi - lo, i * P - lo
            pe.wait(*un[u]["cols"])
            p, r = 2 * g + hd // 2, SLOT * (hd % 2)
            bk = s_banks.take(pe)
            m = pe.mark(lambda e: e.matmul(
                psum[:, bk, 0:w], qT[r:r + ROWS_S, p, i * P:(i + 1) * P], kT[r:r + ROWS_S, p, lo:hi],
                start=True, stop=True))
            js = masked_ring.take(dve)
            dve.wait(m)
            k = dve.mark(lambda e: e.tensor_tensor_reduce(
                masked[:, js, 0:w], psum[:, bk, 0:w], mask[:, P - off:P - off + w], 1.0, MASKED,
                ALU.add, ALU.max, mx[:, b % 2, i, G * g + hd:G * g + hd + 1]))
            masked_ring.give(js, k)
            s_banks.give(bk, k)
            un[u]["mx"] = k

        def u_maxima(u):
            b, g = divmod(u, NG)
            qs = ct[b]["q"]
            m_in = mx[:, b % 2, :, G * g:G * g + G]
            rows_of = q_rowsv[:, qs, :, G * g:G * g + G, :]
            dve.wait(un[u]["mx"])
            k = dve.mark(lambda e: e.tensor_scalar(rows_of[:, :, :, ROWS_S], m_in, -1.0, None, ALU.mult))
            dve.wait(k)
            k = dve.mark(lambda e: e.scalar_tensor_tensor(
                rows_of[:, :, :, ROWS_S + 1], m_in, -1.0, rows_of[:, :, :, ROWS_S].bitcast(F32), ALU.mult, ALU.subtract))
            un[u]["maxima"] = k

        def u_cols_again(u, i):
            b, g = divmod(u, NG)
            p = 2 * g + i
            qs = ct[b]["q"]
            pe.wait(un[u]["maxima"])
            m, k = rows_to_cols(lambda t: q_rows[:, qs, t, p * P:(p + 1) * P], p, qT, act)
            if p == H // 2 - 1:
                q_ring.give(qs, m)
            un[u].setdefault("cols2", []).append(k)

        def u_exp(u, j, hd):
            b, g = divmod(u, NG)
            lo, hi = window(j)
            w = hi - lo
            if hd == 0:
                un[u]["pT", j] = pT_ring.take(act)
                act.wait(k_first_added[0])
            s = un[u]["pT", j]
            pe.wait(*un[u]["cols2"])
            p, r = 2 * g + hd // 2, SLOT * (hd % 2)
            bk = s_banks.take(pe)
            m = pe.mark(lambda e: e.matmul(
                psum[:, bk, 0:w], kT[r:r + ROWS_T, p, j * P:(j + 1) * P], qT[r:r + ROWS_T, p, lo:hi],
                start=True, stop=True))
            act.wait(m)
            k = act.mark(lambda e: e.activation(
                pT[:, s, hd, 0:w], psum[:, bk, 0:w], ACT.Exp, scale=1.0 / E ** 0.5))
            s_banks.give(bk, k)
            if hd < G - 1:
                return
            if j == TPB - 1:
                cols_readers[g] = (m,)
            pool.wait(k)
            if j > 0:
                k = pool.mark(lambda e: e.affine_select(
                    out=pT[:, s, :, 0:P], in_=pT[:, s, :, 0:P], compare_op=ALU.is_ge, fill=0.0, base=0,
                    pattern=[[0, G], [1, P]], channel_multiplier=-1))
            if j < TPB - 1:
                k = pool.mark(lambda e: e.affine_select(
                    out=pT[:, s, :, w - P:w], in_=pT[:, s, :, w - P:w], compare_op=ALU.is_ge, fill=0.0, base=0,
                    pattern=[[0, G], [-1, P]], channel_multiplier=1))
            un[u]["pT", j] = s, k

        def u_values(u, j):
            b, g = divmod(u, NG)
            lo, hi = window(j)
            s, k = un[u]["pT", j]
            vs = ct[b]["v"]
            if j == 0:
                un[u]["o"] = O_BANK.take(pe)
            bk = un[u]["o"]
            pe.wait(k, ct[b]["k_v"])
            for hh in range(G):
                emit = lambda e, hh=hh: e.matmul(
                    psum[32 * hh:32 * hh + 32, bk, lo:hi], v32[:, vs, j, G * g + hh, :], pT[:, s, hh, 0:hi - lo],
                    start=(j == 0), stop=(j == TPB - 1), skip_group_check=True)
                m = pe.mark(emit) if hh == G - 1 else pe.do(emit)
            pT_ring.give(s, m)
            if j == TPB - 1:
                if g == NG - 1:
                    v_ring.give(vs, m)
                oT_ring.take(act)
                act.wait(m)
                k = act.mark(lambda e: e.activation(oT, psum[:, bk, :], ACT.Copy))
                O_BANK.give(bk, k)
                un[u]["oT"] = k

        def u_out(u):
            b, g = divmod(u, NG)
            pe.wait(un[u]["oT"])
            bk = s_banks.take(pe)
            for t in range(TPB):
                emit = lambda e, t=t: e.transpose(psum[:, bk, t * P:(t + 1) * P], oT[:, t * P:(t + 1) * P], ident[:, :])
                m = pe.mark(emit) if t == TPB - 1 else pe.do(emit)
            oT_ring.give(0, m)
            if g == 0:
                o_ring.take(dve)
            v = psum[:, bk, :].rearrange("p (t h f) -> p t h f", t=TPB, h=G)
            rec_ring.take(dve)
            dve.wait(m)
            k = dve.mark(lambda e: e.reciprocal(rec, v[:, :, :, DH]))
            dve.wait(k)
            k = dve.mark(lambda e: e.tensor_tensor(
                o[:, :, G * DH * g:G * DH * (g + 1)].rearrange("p t (h d) -> p t h d", h=G), v[:, :, :, 0:DH],
                rec.rearrange("p t (h i) -> p t h i", i=1).broadcast_to([P, TPB, G, DH]), ALU.mult))
            s_banks.give(bk, k)
            rec_ring.give(0, k)
            ct[b]["o"] = k

        def c_project(b, c):
            pe.wait(ct[b]["o"])
            if c == 0:
                oT2_ring.take(act)
            bk = s_banks.take(pe)
            for t in range(TPB):
                emit = lambda e, t=t: e.transpose(
                    psum[:, bk, t * P:(t + 1) * P], o[:, t, c * P:(c + 1) * P], ident[:, :])
                m = pe.mark(emit) if t == TPB - 1 else pe.do(emit)
            act.wait(m)
            k = act.mark(lambda e: e.activation(oT2[:, c, :], psum[:, bk, :], ACT.Copy))
            s_banks.give(bk, k)
            if c == EC - 1:
                o_ring.give(0, m)
            ct[b]["oT2"] = k

        def c_residual(b, half):
            pe.wait(ct[b]["oT2"])
            bk = s_banks.take(pe)
            for t in (2 * half, 2 * half + 1):
                for c in range(EC):
                    emit = lambda e, t=t, c=c: e.matmul(
                        psum[:, bk, (t % 2) * E:(t % 2 + 1) * E], oT2[:, c, t * P:(t + 1) * P], w_p[:, c, :],
                        start=(c == 0), stop=(c == EC - 1))
                    m = pe.mark(emit) if t % 2 and c else pe.do(emit)
            t0 = b * TPB + 2 * half
            dve.wait(m, k_resid[t0])
            k = dve.mark(lambda e: e.tensor_tensor(
                X[:, t0:t0 + 2, :].rearrange("p t c -> p (t c)"), X[:, t0:t0 + 2, :].rearrange("p t c -> p (t c)"),
                psum[:, bk, :], ALU.add))
            s_banks.give(bk, k)
            k_resid[t0] = k_resid[t0 + 1] = k
            if half == 0:
                return
            oT2_ring.give(0, m)
            ct[b]["projected"] = (m,)
            sp.wait(k)
            ct[b]["stored"] = sp.dma(c_resid, lambda e: e.dma_start(
                resid.rearrange("(b t p) c -> p b t c", p=P, t=TPB)[:, b, :, :], X[:, b * TPB:(b + 1) * TPB, :]))

        def d_norm(b, *tiles):
            c_norm(b, *tiles)
            if tiles[-1] == TPB - 1:
                s, k = ct[b]["xn"]
                ct[b]["xn4"] = s, k, keep_normed(1, b, s, k)

        def d_turn(b):
            s, k, ct[b]["kept"] = ct[b]["xn4"]
            xs = xnT_ring.take(act)
            dve.wait(*xnT_ring.readers.get(xs, ()))
            ct[b]["xnT4"] = xs, transpose_batch(s, k, xnT[:, xs, :, :], s_banks, xn_ring, ct[b]["kept"])

        def d_gate(b):
            xs, ks = ct[b]["xnT4"]
            m, ct[b]["gate"] = gate(1, b, xnT[:, xs, :, :], ks, s_banks)
            xnT_ring.give(xs, m)

        k_w = {}

        def load_expert(x):
            sp.wait(*arena_free(x))
            sp.dma(c_w1[x], lambda e: e.dma_start(w1[:, x, :, :], a["w1"][x].rearrange("(c p) n -> p c n", p=P)))
            k_w[x] = sp.dma(c_w1[x], lambda e: e.dma_start(w2[:, x, :, :], a["w2"][x].rearrange("(c p) n -> p c n", p=P)))

        def arena_free(x):
            if x < 2:
                return q_ring.readers[x]
            if x == 2:
                return k_ring.readers[0]
            if x in (3, 4):
                return cols_readers[NG - 1]
            return v_ring.readers[0] + v_ring.readers[1] + (ct[B - 1]["projected"] if x == NX - 1 else ())

        NU = B * NG
        cc = {}
        PRE = 4 * NG
        for b in range(B):
            s0 = (b - 1) * PRE - 1
            for i in range(TPB * TOP0):
                t, j = b * TPB + i // TOP0, i % TOP0
                at(cc, s0 - 1 + i, 9, fetch, t, j)
                at(cc, s0 + i, 8, add_fetched, t, j)
                if j == TOP0 - 1:
                    at(cc, s0 + i, 8.5, tile_stats, t)
            if b == 0:
                at(cc, s0 + 8, 9, fill_pads)
            at(cc, s0 + 7, 9, norm_scale, b)
            at(cc, s0 + 8, 7, c_norm, b, 0, 1)
            at(cc, s0 + 9, 7, c_norm, b, 2, 3)
            at(cc, s0 + 10, 1.6, c_turn, b)
            for t in range(TPB):
                at(cc, s0 + 11 + t, 3.6, c_qkv, b, t)
                at(cc, s0 + 12 + t, 0.6, c_low, b, t)
        for u in range(NU):
            b, g = divmod(u, NG)
            for n, (of, i) in enumerate((("k", 0), ("k", 1), ("q", 0), ("q", 1))):
                at(cc, 4 * u - 2, n + 1.7, u_cols, u, of, i)
            for i in range(TPB):
                for hd in range(G):
                    at(cc, 4 * u + i, hd, u_scores, u, i, hd)
                    at(cc, 4 * (u + 1) + i + 1, hd + 1.4, u_exp, u, i, hd)
                at(cc, 4 * (u + 1) + i + 3, 1.2, u_values, u, i)
            at(cc, 4 * (u + 1), -1, u_maxima, u)
            for i in range(2):
                at(cc, 4 * (u + 1), 2.9 + i, u_cols_again, u, i)
            at(cc, 4 * (u + 1) + 7, 2.7, u_out, u)
            if g == NG - 1:
                s1 = 4 * (u + 1) + 8
                for c in range(EC):
                    at(cc, s1, 1.7 + c, c_project, b, c)
                for half in range(TPB // 2):
                    at(cc, s1 + 1, 1.7 + half, c_residual, b, half)
                for t in range(TPB):
                    at(cc, s1 + 1 + t // 2, 8, tile_stats, b * TPB + t)
                at(cc, s1 + 2, 9, norm_scale, b)
                at(cc, s1 + 3, 7, d_norm, b, 0, 1)
                at(cc, s1 + 4, 7, d_norm, b, 2, 3)
                at(cc, s1 + 5, 1.6, d_turn, b)
                at(cc, s1 + 5, 9, d_gate, b)
        end = 4 * NU
        at(cc, end - 4, 10, load_expert, 2)
        at(cc, end - 12, 10, load_expert, (B - 2) % 2)
        at(cc, end + 1, 10, load_expert, (B - 1) % 2)
        for x in (3, 4):
            at(cc, end + 5, 10, load_expert, x)
        for x in (5, 6, 7):
            at(cc, end + 10, 10, load_expert, x)
        run(cc)

        for _ in find_rows(1, ct[B - 1]["gate"], s_banks, 4096, 0, [ct[b]["kept"] for b in (B - 2, B - 1)]):
            pass
        k_expert1, k_token1 = found["expert", 1], found["token", 1]

        def experts1():
            h = carve(work, 0, 2, HID)
            hT = carve(work, 2048, 2, HID)
            xs = carve(work, 4096, 3, E)
            xsT = carve(work, 4864, 2, E)
            xr = carve(work, 5376, 4, E)
            y = carve(work, 6400, 3, E)
            rx, rt, rh, ra, rr, ry = (Ring(list(range(n))) for n in (3, 2, 2, 2, 4, 3))
            x_banks, u_banks, t_banks, o_banks = banks([6]), banks([(0, 1), (2, 3)]), banks([(4, 5)]), banks([7])
            it = [dict() for _ in range(NBLK1)]
            k_done = {}
            kept = [k_token1, k_expert1, ct[B - 1]["stored"]] + [ct[b]["kept"] for b in (B - 2, B - 1)]
            HC = HID // P

            def load(b):
                it[b]["xs"] = load_rows(1, b, rx, xs, kept)

            def load_residual(b):
                s = rr.take(pool)
                it[b]["xr"] = s, pool.dma(c_xrow[s], lambda e: e.indirect_dma_start(
                    out=xr[:, s, :], out_offset=None, in_=resid,
                    in_offset=bass.IndirectOffsetOnAxis(ap=token_of[:, 1, b:b + 1], axis=0)))

            def turn(b):
                it[b]["xsT"] = turn_rows(*it[b]["xs"], xs, xsT, x_banks, rt, rx)

            def up(b):
                q, k = it[b]["xsT"]
                pe.wait(k, k_w[min(b, NX - 1)], k_expert1)
                pair = u_banks.take(pe)

                def emit_up(e):
                    x = e.value_load(blk_expert[0:1, 1, b:b + 1], min_val=0, max_val=NX - 1)
                    for u in range(2):
                        for c in range(EC):
                            m = e.matmul(psum[:, pair[u], :], xsT[:, q, c * P:(c + 1) * P],
                                         w1[:, bass.ds(x, 1), c, u * N:(u + 1) * N],
                                         start=(c == 0), stop=(c == EC - 1))
                    return m
                m = pe.mark(emit_up)
                rt.give(q, m)
                s = rh.take(act)
                act.wait(m)
                k = act.mark(lambda e: e.activation(
                    h[:, s, :], psum[:, pair[0]:pair[0] + 2, :].rearrange("p a n -> p (a n)"), ACT.Gelu_apprx_tanh))
                u_banks.give(pair, k)
                it[b]["h"] = s, k

            def turn_h(b):
                s, k = it[b]["h"]
                pe.wait(k)
                pair = t_banks.take(pe)
                for c in range(HC):
                    emit = lambda e, c=c: e.transpose(psum[:, pair[c // 4], (c % 4) * P:(c % 4 + 1) * P],
                                                      h[:, s, c * P:(c + 1) * P], ident[:, :])
                    m = pe.mark(emit) if c % 4 == 3 else pe.do(emit)
                    if c == 3:
                        m0 = m
                rh.give(s, m)
                q = ra.take(dve)
                dve.wait(m0)
                kd = dve.mark(lambda e: e.tensor_copy(hT[:, q, 0:N], psum[:, pair[0], :]))
                dve.wait(m)
                kd = dve.mark(lambda e: e.tensor_copy(hT[:, q, N:2 * N], psum[:, pair[1], :]))
                t_banks.give(pair, kd)
                it[b]["hT"] = q, kd

            def down(b):
                q, k = it[b]["hT"]
                pe.wait(k)
                bk = o_banks.take(pe)

                def emit_down(e):
                    x = e.value_load(blk_expert[0:1, 1, b:b + 1], min_val=0, max_val=NX - 1)
                    for c in range(HC):
                        m = e.matmul(psum[:, bk, 0:E], hT[:, q, c * P:(c + 1) * P], w2[:, bass.ds(x, 1), c, :],
                                     start=(c == 0), stop=(c == HC - 1))
                    return m
                m = pe.mark(emit_down)
                ra.give(q, m)
                r, k = it[b]["xr"]
                s = ry.take(dve)
                dve.wait(m, k)
                k = dve.mark(lambda e: e.tensor_tensor(y[:, s, :], psum[:, bk, 0:E], xr[:, r, :], ALU.add))
                o_banks.give(bk, k)
                rr.give(r, k)
                pool.wait(k)
                k_done[s] = pool.dma(c_out[s], lambda e: e.indirect_dma_start(
                    out=out.rearrange("b n c -> (b n) c"),
                    out_offset=bass.IndirectOffsetOnAxis(ap=token_out[:, b:b + 1], axis=0),
                    in_=y[:, s, :], in_offset=None, bounds_check=NT * P - 1, oob_is_err=False))
                ry.give(s, k_done[s])

            pipeline(NBLK1, [load, lambda b: None, lambda b: (turn(b), load_residual(b)), up, turn_h, down])
            return list(k_done.values())

        sp.wait(*experts1())

        @block.tensor
        def _(e):
            for f in pe.todo:
                f(e)

        @block.scalar
        def _(e):
            for f in act.todo:
                f(e)

        @block.vector
        def _(e):
            for f in dve.todo:
                f(e)

        @block.gpsimd
        def _(e):
            for f in pool.todo:
                f(e)

        @block.sync
        def _(e):
            for f in sp.todo:
                f(e)


def kernel(**inputs):
    import numpy as np
    import concourse.bacc as bacc
    from concourse.bass_utils import run_bass_kernel_spmd

    g = {k: np.asarray(v) for k, v in inputs.items()}
    arrays = {
        "x": g["L0_attn_x"],
        "wkvT": np.concatenate([g["L0_attn_wk"], g["L0_attn_wv"]]).T,
        "wqT": g["L0_attn_wq"].T,
        "woT": g["L0_attn_wo"].T,
        "gate0T": g["L0_ffn_gate_w"].T,
        "wg": g["L0_ffn_wg"], "wu": g["L0_ffn_wu"], "wd": g["L0_ffn_wd"],
        "swg": g["L0_ffn_swg"], "swu": g["L0_ffn_swu"], "swd": g["L0_ffn_swd"],
        "wqkvT": np.concatenate([g["L1_attn_Wq"], g["L1_attn_Wk"], g["L1_attn_Wv"]]).T,
        "bqkv": np.concatenate([g["L1_attn_bq"], g["L1_attn_bk"], g["L1_attn_bv"]]),
        "wpT": g["L1_attn_Wp"].T, "bp": g["L1_attn_bp"],
        "w1": g["L1_ffn_W1"], "w2": g["L1_ffn_W2"], "gate1": g["L1_ffn_Wg"], "bg": g["L1_ffn_bg"],
    }
    arrays = {f"in_{k}": np.ascontiguousarray(v) for k, v in arrays.items()}
    nc = bacc.Bacc("TRN2", target_bir_lowering=False, num_devices=1)
    aps = {k[3:]: nc.dram_tensor(k, v.shape, mybir.dt.from_np(v.dtype), kind="ExternalInput").ap()
           for k, v in arrays.items()}
    out = nc.dram_tensor("out", arrays["in_x"].shape, F32, kind="ExternalOutput").ap()
    build(nc, aps, out)
    return run_bass_kernel_spmd(nc, [arrays], core_ids=[0]).results[0]["out"]
```
